# Optimizing a Trainium2 kernel written in Bass

```python
import numpy as np
import jax
import jax.numpy as jnp

def _softmax(x, axis=-1):
    return jax.nn.softmax(x, axis=axis)

def _gelu(x):
    return jax.nn.gelu(x, approximate=True)

def _silu(x):
    return jax.nn.silu(x)

def _sigmoid(x):
    return jax.nn.sigmoid(x)

def _layernorm(x, axis=-1, eps=1e-05):
    m = jnp.mean(x, axis=axis, keepdims=True)
    v = jnp.var(x, axis=axis, keepdims=True)
    return (x - m) / jnp.sqrt(v + eps)

def _scatter_add(tgt, idx, src, axis=0):
    return tgt.at[idx].add(src)

def _segment_sum(src, seg, n):
    return jax.ops.segment_sum(src, seg, n)
kernel_name = 'mk_cond_resid_d2_seqx_r8_bca9c8'

def setup_inputs(seed: int=0):
    np.random.seed(seed)
    _w = jnp.asarray

    def _rec_inputs():
        import jax
        import jax.numpy as jnp
        _rk = jax.random.key(seed)
        x = -0.000125 + 0.9999 * jax.random.normal(jax.random.fold_in(_rk, 1), (64, 32, 512), jnp.float32)
        _lenS = 32 - jax.random.randint(jax.random.fold_in(_rk, 7), (64,), 0, max(1, 32 // 4) + 1, jnp.int32)
        _lenS2 = 32 - jax.random.randint(jax.random.fold_in(_rk, 8), (64,), 0, max(1, 32 // 4) + 1, jnp.int32)
        itok_B_6_15 = jax.random.randint(jax.random.fold_in(_rk, 11), (64,), 6, 16, jnp.int32)
        itok_B_0_23 = jax.random.randint(jax.random.fold_in(_rk, 12), (64,), 0, 24, jnp.int32)
        return (x, itok_B_6_15, itok_B_0_23)
    x, itok_B_6_15, itok_B_0_23 = _rec_inputs()

    def _L0_cond_setup():
        import jax, jax.numpy as jnp
        import numpy as np
        B, S, D_IN, D_OUT = (4, 256, 512, 512)
        RANK, MAX_LORAS = (16, 32)
        key = jax.random.key(seed)
        ks = jax.random.split(key, 6)
        x = jax.random.normal(ks[0], (B, S, D_IN), dtype=jnp.float32)
        adapter_ids = jax.random.randint(ks[1], (B,), 0, MAX_LORAS)
        base_weight = jax.random.normal(ks[2], (D_OUT, D_IN), dtype=jnp.float32) * D_IN ** (-0.5)
        base_bias = jax.random.normal(ks[3], (D_OUT,), dtype=jnp.float32) * 0.01
        lora_A_w = jax.random.normal(ks[4], (MAX_LORAS, RANK, D_IN), dtype=jnp.float32) * D_IN ** (-0.5)
        lora_B_w = jax.random.normal(ks[5], (MAX_LORAS, D_OUT, RANK), dtype=jnp.float32) * RANK ** (-0.5)
        return {'x': x, 'adapter_ids': adapter_ids, 'base_weight': base_weight, 'base_bias': base_bias, 'lora_A_w': lora_A_w, 'lora_B_w': lora_B_w}
    _L0_cond_all = _L0_cond_setup()
    _L0_cond_in = {k: v for k, v in _L0_cond_all.items() if k in ('base_weight', 'base_bias', 'lora_A_w', 'lora_B_w')}
    del _L0_cond_all

    def _L1_cond_setup():
        import jax, jax.numpy as jnp
        import numpy as np
        R = 16
        ALPHA = 32
        SCALING = ALPHA / R
        SLOTS = 32
        IN_F = 512
        OUT_F = 512
        B, T = (8, 128)
        key = jax.random.key(seed)
        k1, k2, k3, k4, k5, k6 = jax.random.split(key, 6)
        x = jax.random.normal(k1, (B, T, IN_F), dtype=jnp.float32)
        adapter_mapping = jax.random.randint(k2, (B,), 0, SLOTS, dtype=jnp.int32)
        W = jax.random.normal(k3, (OUT_F, IN_F), dtype=jnp.float32) * 0.02
        b = jax.random.normal(k4, (OUT_F,), dtype=jnp.float32) * 0.02
        lora_As = jax.random.normal(k5, (SLOTS, IN_F, R), dtype=jnp.float32) * 0.02
        lora_Bs = jax.random.normal(k6, (SLOTS, R, OUT_F), dtype=jnp.float32) * 0.02
        return {'x': x, 'adapter_mapping': adapter_mapping, 'W': W, 'b': b, 'lora_As': lora_As, 'lora_Bs': lora_Bs}
    _L1_cond_all = _L1_cond_setup()
    _L1_cond_in = {k: v for k, v in _L1_cond_all.items() if k in ('W', 'b', 'lora_As', 'lora_Bs')}
    del _L1_cond_all
    return {'x': x, 'itok_B_6_15': itok_B_6_15, 'itok_B_0_23': itok_B_0_23, 'L0_cond_base_weight': _L0_cond_in['base_weight'], 'L0_cond_base_bias': _L0_cond_in['base_bias'], 'L0_cond_lora_A_w': _L0_cond_in['lora_A_w'], 'L0_cond_lora_B_w': _L0_cond_in['lora_B_w'], 'L1_cond_W': _L1_cond_in['W'], 'L1_cond_b': _L1_cond_in['b'], 'L1_cond_lora_As': _L1_cond_in['lora_As'], 'L1_cond_lora_Bs': _L1_cond_in['lora_Bs']}

def reference(x, itok_B_6_15, itok_B_0_23, L0_cond_base_weight, L0_cond_base_bias, L0_cond_lora_A_w, L0_cond_lora_B_w, L1_cond_W, L1_cond_b, L1_cond_lora_As, L1_cond_lora_Bs):
    import jax
    import jax.numpy as jnp

    def _L0_cond_ref(x, adapter_ids, base_weight, base_bias, lora_A_w, lora_B_w):
        import jax, jax.numpy as jnp
        import numpy as np
        B, S, D_IN, D_OUT = (4, 256, 512, 512)
        RANK, MAX_LORAS = (16, 32)
        result = jnp.einsum('bsd,od->bso', x, base_weight) + base_bias
        A = lora_A_w[adapter_ids]
        Bw = lora_B_w[adapter_ids]
        h = jnp.einsum('bsd,brd->bsr', x, A)
        lora_out = jnp.einsum('bsr,bor->bso', h, Bw)
        result = result + lora_out
        return result.astype(x.dtype)

    def _L1_cond_ref(x, adapter_mapping, W, b, lora_As, lora_Bs):
        import jax, jax.numpy as jnp
        import numpy as np
        R = 16
        ALPHA = 32
        SCALING = ALPHA / R
        SLOTS = 32
        IN_F = 512
        OUT_F = 512
        B, T = (8, 128)
        base_out = jnp.einsum('bti,oi->bto', x, W) + b
        A = lora_As[adapter_mapping]
        Bm = lora_Bs[adapter_mapping]
        lora_h = jnp.einsum('bti,bir->btr', x, A)
        lora_out = jnp.einsum('btr,bro->bto', lora_h, Bm)
        return base_out + lora_out * SCALING
    x = x + _L0_cond_ref(x, itok_B_6_15, L0_cond_base_weight, L0_cond_base_bias, L0_cond_lora_A_w, L0_cond_lora_B_w)
    x = x + _L1_cond_ref(x, itok_B_0_23, L1_cond_W, L1_cond_b, L1_cond_lora_As, L1_cond_lora_Bs)
    return x

_drawn_inputs = setup_inputs


def setup_inputs(seed=0):
    import zlib

    import numpy as np

    out = dict(_drawn_inputs(seed))
    spreads = {}
    factors = {'L0_cond_base_bias': 8.0, 'L1_cond_b': 6.394}
    for name, (base, spread) in spreads.items():
        noise = np.random.default_rng([zlib.crc32(name.encode()), seed]).standard_normal(out[name].shape)
        drawn = base * np.exp(spread * noise) if base else spread * noise
        out[name] = jnp.asarray(drawn.astype(out[name].dtype))
    for name, factor in factors.items():
        out[name] = (out[name] * factor).astype(out[name].dtype)
    return out
```

```python
from contextlib import ExitStack

import concourse.bass as bass
from concourse import mybir

F32 = mybir.dt.float32
F32R = mybir.dt.float32r
I32 = mybir.dt.int32
U32 = mybir.dt.uint32
ALU = mybir.AluOpType

P = 128
BATCHES, SEQ, FEATURES = 64, 32, 512
ADAPTERS, RANK = 32, 16
TOKENS = BATCHES * SEQ
SLICES = FEATURES // P
CHUNK = 512
CHUNKS = TOKENS // CHUNK
GROUP_BATCHES = P // RANK
GROUP = GROUP_BATCHES * SEQ
GROUPS = CHUNK // GROUP
CHUNK_BATCHES = CHUNK // SEQ
LAYERS = 2
LORA_SCALE = (1.0, 2.0)
DMA = 16
HI, LO = 0, 1
PASSES = ((HI, HI), (HI, LO), (LO, HI))


def lora_layers_kernel(nc, xT, ids, ids_by_row, w, bias, lora_a, lora_b, outT):
    with ExitStack() as ctx:
        def sb(name, shape, dt=F32):
            return ctx.enter_context(nc.sbuf_tensor(name, shape, dt))

        def psum(name, shape):
            return ctx.enter_context(nc.psum_tensor(name, shape, F32))

        def sem(name):
            return ctx.enter_context(nc.semaphore(name))

        def per_layer(make, name, *args):
            return [make(f"{name}{n}", *args) for n in range(LAYERS)]

        x = sb("x_all", [P, SLICES, TOKENS])
        x_parts = [[sb(f"x{n}_{part}", [P, SLICES, CHUNK], F32R) for part in ("hi", "lo")]
                   for n in range(LAYERS)]
        w_raw = per_layer(sb, "w_raw", [P, SLICES, FEATURES])
        w_parts = [[sb(f"w{n}_{part}", [P, SLICES, SLICES, P], F32R) for part in ("hi", "lo")]
                   for n in range(LAYERS)]
        bias_sb = sb("bias_sb", [P, LAYERS * SLICES])
        a_raw = per_layer(sb, "a_raw", [P, CHUNK_BATCHES, SLICES, RANK])
        a_parts = [[sb(f"a{n}_{part}", [P, SLICES, CHUNK_BATCHES, RANK], F32R) for part in ("hi", "lo")]
                   for n in range(LAYERS)]
        b_raw = per_layer(sb, "b_raw", [P, CHUNKS * GROUPS, FEATURES])
        b_parts = [[sb(f"b{n}_{part}", [P, GROUPS, FEATURES], F32R) for part in ("hi", "lo")]
                   for n in range(LAYERS)]
        h_masked = sb("h_masked", [P, GROUPS, GROUP])
        h_parts = [sb(f"h_{part}", [P, GROUPS, GROUP], F32R) for part in ("hi", "lo")]
        own_batch = sb("own_batch", [P, GROUP_BATCHES, SEQ])
        ids_sb = sb("ids_sb", [1, LAYERS * BATCHES], I32)
        ids_row_sb = sb("ids_row_sb", [P, LAYERS * CHUNKS * GROUPS], I32)
        partition = sb("partition", [P, 1], I32)
        rank_row = sb("rank_row", [P, 1], I32)
        rank_row_f = sb("rank_row_f", [P, 1])
        b_index = sb("b_index", [P, LAYERS * CHUNKS * GROUPS], U32)

        out_bank = [psum(f"out_bank{m}", [P, CHUNK]) for m in range(SLICES)]
        h_bank = [psum(f"h_bank{g}", [P, GROUP]) for g in range(GROUPS)]

        ids_landed = sem("ids_landed")
        ids_row_landed = sem("ids_row_landed")
        bias_landed = sem("bias_landed")
        w0_landed = [sem(f"w0_landed{k}") for k in range(SLICES)]
        w1_landed = sem("w1_landed")
        x0_landed = [sem(f"x0_landed{k}") for k in range(SLICES)]
        x1_landed = sem("x_chunk1_landed")
        x_rest_landed = sem("x_rest_landed")
        a_landed = per_layer(sem, "a_landed")
        b_first_landed = per_layer(sem, "b_first_landed")
        b_rest_landed = per_layer(sem, "b_rest_landed")
        stored = sem("stored")
        index_steps = sem("index_steps")
        mask_steps = sem("mask_steps")
        w_hi = per_layer(sem, "w_hi")
        w_lo = per_layer(sem, "w_lo")
        x_hi = per_layer(sem, "x_hi")
        x_lo = per_layer(sem, "x_lo")
        a_hi = per_layer(sem, "a_hi")
        a_lo = per_layer(sem, "a_lo")
        b_hi = per_layer(sem, "b_hi")
        b_lo = per_layer(sem, "b_lo")
        h_mask_done = sem("h_mask_done")
        h_hi = sem("h_hi")
        h_lo = sem("h_lo")
        bank_evicted = sem("bank_evicted")
        x_read = per_layer(sem, "x_read")
        a_read = per_layer(sem, "a_read")
        h_ready = sem("h_ready")
        bank_ready = sem("bank_ready")

        xT_v = xT.rearrange("(p k) t -> p k t", k=SLICES)
        outT_v = outT.rearrange("(p k) t -> p k t", k=SLICES)
        w_v = [v.rearrange("(p k) m q -> p k (m q)", k=SLICES) for v in w]

        def chunk_of(c):
            return bass.ds(c * CHUNK, CHUNK)

        def f32(ap):
            return ap.bitcast(F32)

        def chunk_after_next(j):
            return nc.s_assert_within(j + 2, 2, CHUNKS - 1, 
                                      skip_runtime_bounds_check_because="the branch holds it")

        block = ctx.enter_context(nc.Block())

        @block.sync
        def _(sp):
            sp.dma_start(ids_sb[:], ids).then_inc(ids_landed, DMA)
            for k in range(SLICES):
                sp.dma_start(w_raw[0][:, k, :], w_v[0][:, k, :]).then_inc(w0_landed[k], DMA)
            sp.wait_ge(ids_landed, DMA)
            id_regs = [sp.alloc_register(f"adapter_id{b}") for b in range(CHUNK_BATCHES)]

            def gather_a(n, c):
                sp.load(id_regs, ids_sb[0:1, bass.ds(n * BATCHES + c * CHUNK_BATCHES, CHUNK_BATCHES)])
                for b in range(CHUNK_BATCHES):
                    adapter = sp.snap(id_regs[b], min_val=0, max_val=ADAPTERS - 1)
                    sp.dma_start(a_raw[n][:, b, :, :].rearrange("p k r -> p (k r)"),
                                 lora_a[n][bass.ds(adapter, 1)].rearrange("a p e -> (a p) e")
                                 ).then_inc(a_landed[n], DMA)

            for n in range(LAYERS):
                gather_a(n, 0)
            with sp.Fori(1, CHUNKS) as c:
                for n in range(LAYERS):
                    sp.wait_ge(a_lo[n], c)
                    gather_a(n, c)

        @block.gpsimd
        def _(pool):
            pool.dma_start(ids_row_sb[:], ids_by_row).then_inc(ids_row_landed, DMA)
            pool.iota(partition[:], pattern=[[0, 1]], base=0, channel_multiplier=1).then_inc(index_steps, 1)
            pool.memset(own_batch[:], 1.0).then_inc(mask_steps, 1)
            pool.wait_ge(index_steps, 4)

            def gather_b(n, g, landed):
                col = n * CHUNKS * GROUPS + g
                pool.indirect_dma_start(
                    out=b_raw[n][:, g, :], out_offset=None, in_=lora_b[n],
                    in_offset=bass.IndirectOffsetOnAxis(ap=b_index[:, col:col + 1], axis=0),
                ).then_inc(landed, DMA)

            for g in range(GROUPS):
                gather_b(0, g, b_first_landed[0])
            pool.wait_ge(mask_steps, 1)
            pool.affine_select(out=own_batch[:], in_=own_batch[:], compare_op=ALU.is_ge, fill=0.0, base=0,
                               pattern=[[-RANK, GROUP_BATCHES], [0, SEQ]],
                               channel_multiplier=1).then_inc(mask_steps, 1)
            pool.wait_ge(mask_steps, 2)
            pool.affine_select(out=own_batch[:], in_=own_batch[:], compare_op=ALU.is_ge, fill=0.0,
                               base=RANK - 1, pattern=[[RANK, GROUP_BATCHES], [0, SEQ]],
                               channel_multiplier=-1).then_inc(mask_steps, 1)
            for g in range(GROUPS, CHUNKS * GROUPS):
                gather_b(0, g, b_rest_landed[0])
            for g in range(GROUPS):
                gather_b(1, g, b_first_landed[1])
            for g in range(GROUPS, CHUNKS * GROUPS):
                gather_b(1, g, b_rest_landed[1])

            def low_parts(n, c):
                pool.wait_ge(a_hi[n], c + 1)
                pool.tensor_tensor(a_parts[n][LO][:], a_raw[n][:].rearrange("p b k r -> p k b r"),
                                   f32(a_parts[n][HI][:]), ALU.subtract).then_inc(a_lo[n], 1)
                pool.wait_ge(b_hi[n], c + 1)
                pool.tensor_tensor(b_parts[n][LO][:], b_raw[n][:, bass.ds(c * GROUPS, GROUPS), :],
                                   f32(b_parts[n][HI][:]), ALU.subtract).then_inc(b_lo[n], 1)

            low_parts(0, 1)
            with pool.Fori(0, CHUNKS - 1) as j:
                low_parts(1, j)
                with pool.If(j < CHUNKS - 2):
                    low_parts(0, chunk_after_next(j))
            low_parts(1, CHUNKS - 1)

        @block.scalar
        def _(act):
            for k in range(SLICES):
                act.dma_start(x[:, k, 0:CHUNK], xT_v[:, k, 0:CHUNK]).then_inc(x0_landed[k], DMA)
            act.dma_start(bias_sb[:], bias).then_inc(bias_landed, DMA)
            act.dma_start(x[:, :, CHUNK:2 * CHUNK], xT_v[:, :, CHUNK:2 * CHUNK]).then_inc(x1_landed, DMA)
            act.dma_start(w_raw[1][:], w_v[1]).then_inc(w1_landed, DMA)
            for c in range(2, CHUNKS):
                act.dma_start(x[:, :, c * CHUNK:(c + 1) * CHUNK],
                              xT_v[:, :, c * CHUNK:(c + 1) * CHUNK]).then_inc(x_rest_landed, DMA)

            def x_high(n, c, k):
                nc.scalar.copy(x_parts[n][HI][:, k, :], x[:, k, chunk_of(c)]).then_inc(x_hi[n], 1)

            def a_high(n):
                nc.scalar.copy(a_parts[n][HI][:], a_raw[n][:].rearrange("p b k r -> p k b r")
                               ).then_inc(a_hi[n], 1)

            def b_high(n, c):
                nc.scalar.copy(b_parts[n][HI][:], b_raw[n][:, bass.ds(c * GROUPS, GROUPS), :]
                               ).then_inc(b_hi[n], 1)

            def h_high(q):
                for g in range(GROUPS):
                    act.wait_ge(h_mask_done, GROUPS * q + g + 1)
                    nc.scalar.copy(h_parts[HI][:, g, :], h_masked[:, g, :]).then_inc(h_hi, 1)

            def store(c, q):
                for m in range(SLICES):
                    act.wait_ge(bank_evicted, SLICES * q + m + 1)
                    act.dma_start(outT_v[:, m, chunk_of(c)], x[:, m, chunk_of(c)]).then_inc(stored, DMA)

            for k in range(SLICES):
                act.wait_ge(w0_landed[k], DMA)
                nc.scalar.copy(w_parts[0][HI][:, k, :, :], w_raw[0][:, k, :]).then_inc(w_hi[0], 1)
                act.wait_ge(x0_landed[k], DMA)
                x_high(0, 0, k)
            act.wait_ge(b_first_landed[0], DMA * GROUPS)
            b_high(0, 0)
            act.wait_ge(a_landed[0], DMA * CHUNK_BATCHES)
            a_high(0)
            act.wait_ge(w1_landed, DMA)
            for k in range(SLICES):
                nc.scalar.copy(w_parts[1][HI][:, k, :, :], w_raw[1][:, k, :]).then_inc(w_hi[1], 1)
            act.wait_ge(x1_landed, DMA)
            h_high(0)
            for k in range(SLICES):
                act.wait_ge(x_read[0], k + 1)
                x_high(0, 1, k)
            act.wait_ge(a_landed[0], 2 * DMA * CHUNK_BATCHES)
            act.wait_ge(a_read[0], 1)
            a_high(0)
            act.wait_ge(b_rest_landed[0], DMA * GROUPS * (CHUNKS - 1))
            act.wait_ge(bank_ready, SLICES)
            b_high(0, 1)
            act.wait_ge(x_rest_landed, DMA * (CHUNKS - 2))
            act.wait_ge(b_first_landed[1], DMA * GROUPS)
            act.wait_ge(b_rest_landed[1], DMA * GROUPS * (CHUNKS - 1))

            def prepare_l1(c, x1_written, c_is_first):
                for k in range(SLICES):
                    act.wait_ge(bank_evicted, x1_written + k + 1)
                    x_high(1, c, k)

            with act.Fori(0, CHUNKS - 1) as j:
                act.wait_ge(bank_ready, SLICES * (2 * j + 1))
                for k in range(SLICES):
                    if k == 0:
                        act.wait_ge(bank_evicted, SLICES * (2 * j + 1))
                    x_high(1, j, k)
                act.wait_ge(a_landed[1], DMA * CHUNK_BATCHES * (j + 1))
                a_high(1)
                b_high(1, j)
                h_high(2 * j + 1)
                with act.If(j < CHUNKS - 2):
                    act.wait_ge(bank_ready, SLICES * (2 * j + 2))
                    for k in range(SLICES):
                        x_high(0, chunk_after_next(j), k)
                    act.wait_ge(a_landed[0], DMA * CHUNK_BATCHES * (j + 3))
                    a_high(0)
                    b_high(0, chunk_after_next(j))
                h_high(2 * j + 2)
                store(j, 2 * j + 2)
            for k in range(SLICES):
                act.wait_ge(x_read[1], SLICES * (CHUNKS - 1) - SLICES + k + 1)
                x_high(1, CHUNKS - 1, k)
            act.wait_ge(a_landed[1], DMA * CHUNK_BATCHES * CHUNKS)
            a_high(1)
            act.wait_ge(bank_ready, SLICES * (2 * CHUNKS - 1))
            b_high(1, CHUNKS - 1)
            h_high(2 * CHUNKS - 1)
            store(CHUNKS - 1, 2 * CHUNKS - 1)
            act.wait_ge(stored, DMA * SLICES * CHUNKS)

        @block.vector
        def _(dve):
            dve.wait_ge(index_steps, 1)
            dve.tensor_scalar(rank_row[:], partition[:], RANK - 1, None, ALU.bitwise_and
                              ).then_inc(index_steps, 1)
            dve.wait_ge(index_steps, 2)
            dve.tensor_copy(rank_row_f[:], rank_row[:]).then_inc(index_steps, 1)
            dve.wait_ge(index_steps, 3)
            dve.wait_ge(ids_row_landed, DMA)
            dve.tensor_scalar(b_index[:], ids_row_sb[:], float(RANK), rank_row_f[:, 0:1], ALU.mult, ALU.add
                              ).then_inc(index_steps, 1)

            def w_low(n, k):
                dve.wait_ge(w_hi[n], k + 1)
                dve.tensor_tensor(w_parts[n][LO][:, k, :, :].rearrange("p m q -> p (m q)"),
                                  w_raw[n][:, k, :],
                                  f32(w_parts[n][HI][:, k, :, :]).rearrange("p m q -> p (m q)"),
                                  ALU.subtract).then_inc(w_lo[n], 1)

            def x_low(n, c, k):
                dve.wait_ge(x_hi[n], SLICES * c + k + 1)
                dve.tensor_tensor(x_parts[n][LO][:, k, :], x[:, k, chunk_of(c)],
                                  f32(x_parts[n][HI][:, k, :]), ALU.subtract).then_inc(x_lo[n], 1)

            def mask_and_low(n, q):
                for g in range(GROUPS):
                    dve.wait_ge(h_ready, GROUPS * q + g + 1)
                    dve.scalar_tensor_tensor(
                        out=h_masked[:, g, :], in0=h_bank[g][:], scalar=LORA_SCALE[n],
                        in1=own_batch[:].rearrange("p b s -> p (b s)"), op0=ALU.mult, op1=ALU.mult,
                    ).then_inc(h_mask_done, 1)
                for g in range(GROUPS):
                    dve.wait_ge(h_hi, GROUPS * q + g + 1)
                    dve.tensor_tensor(h_parts[LO][:, g, :], h_masked[:, g, :],
                                      f32(h_parts[HI][:, g, :]), ALU.subtract).then_inc(h_lo, 1)

            def evict(n, c, q, m):
                dve.wait_ge(bank_ready, SLICES * q + m + 1)
                col = n * SLICES + m
                dve.scalar_tensor_tensor(
                    out=x[:, m, chunk_of(c)], in0=out_bank[m][:], scalar=bias_sb[:, col:col + 1],
                    in1=x[:, m, chunk_of(c)], op0=ALU.add, op1=ALU.add).then_inc(bank_evicted, 1)

            for k in range(SLICES):
                w_low(0, k)
                x_low(0, 0, k)
            dve.wait_ge(b_hi[0], 1)
            dve.tensor_tensor(b_parts[0][LO][:], b_raw[0][:, 0:GROUPS, :], f32(b_parts[0][HI][:]),
                              ALU.subtract).then_inc(b_lo[0], 1)
            dve.wait_ge(a_hi[0], 1)
            dve.tensor_tensor(a_parts[0][LO][:], a_raw[0][:].rearrange("p b k r -> p k b r"),
                              f32(a_parts[0][HI][:]), ALU.subtract).then_inc(a_lo[0], 1)
            dve.wait_ge(mask_steps, 3)
            dve.wait_ge(bias_landed, DMA)
            mask_and_low(0, 0)
            for k in range(SLICES - 1):
                x_low(0, 1, k)
            evict(0, 0, 0, 0)
            x_low(0, 1, SLICES - 1)
            for m in range(1, SLICES):
                evict(0, 0, 0, m)
            for k in range(SLICES):
                w_low(1, k)
            with dve.Fori(0, CHUNKS - 1) as j:
                for k in range(SLICES):
                    x_low(1, j, k)
                mask_and_low(0, 2 * j + 1)
                for m in range(SLICES):
                    evict(0, j + 1, 2 * j + 1, m)
                with dve.If(j < CHUNKS - 2):
                    for k in range(SLICES):
                        x_low(0, chunk_after_next(j), k)
                mask_and_low(1, 2 * j + 2)
                for m in range(SLICES):
                    evict(1, j, 2 * j + 2, m)
            for k in range(SLICES):
                x_low(1, CHUNKS - 1, k)
            mask_and_low(1, 2 * CHUNKS - 1)
            for m in range(SLICES):
                evict(1, CHUNKS - 1, 2 * CHUNKS - 1, m)

        @block.tensor
        def _(pe):
            def base(n, m, k, part_of_w, part_of_x, first):
                return nc.tensor.matmul(out_bank[m][:], w_parts[n][part_of_w][:, k, m, :],
                                        x_parts[n][part_of_x][:, k, :], start=first, stop=False)

            def lora_down(n, g, k):
                b0 = g * GROUP_BATCHES
                for i, (part_of_a, part_of_x) in enumerate(PASSES):
                    last = nc.tensor.matmul(
                        h_bank[g][:],
                        a_parts[n][part_of_a][:, k, b0:b0 + GROUP_BATCHES, :].rearrange("p b r -> p (b r)"),
                        x_parts[n][part_of_x][:, k, g * GROUP:(g + 1) * GROUP],
                        start=(k == 0 and i == 0), stop=(k == SLICES - 1 and i == len(PASSES) - 1))
                return last

            def lora_up(n, m):
                for g in range(GROUPS):
                    for i, (part_of_b, part_of_h) in enumerate(PASSES):
                        last = nc.tensor.matmul(
                            out_bank[m][:, g * GROUP:(g + 1) * GROUP],
                            b_parts[n][part_of_b][:, g, m * P:(m + 1) * P], h_parts[part_of_h][:, g, :],
                            start=False, stop=(g == GROUPS - 1 and i == len(PASSES) - 1))
                last.then_inc(bank_ready, 1)

            def wait_for_up(n, c, q):
                pe.wait_ge(b_lo[n], c + 1)
                pe.wait_ge(h_lo, GROUPS * (q + 1))

            def phase(n, c, q):
                for m in range(SLICES):
                    pe.wait_ge(bank_evicted, SLICES * (q - 1) + m + 1)
                    for k in range(SLICES):
                        if m == 0:
                            pe.wait_ge(x_lo[n], SLICES * c + k + 1)
                        for i, (part_of_w, part_of_x) in enumerate(PASSES):
                            last = base(n, m, k, part_of_w, part_of_x, k == 0 and i == 0)
                        if m == SLICES - 1:
                            last.then_inc(x_read[n], 1)
                    if m == 0:
                        pe.wait_ge(a_lo[n], c + 1)
                        for g in range(GROUPS):
                            pe.wait_ge(h_mask_done, GROUPS * (q - 1) + g + 1)
                            for k in range(SLICES):
                                last = lora_down(n, g, k)
                            last.then_inc(h_ready, 1)
                        pe.wait_ge(h_ready, GROUPS * (q + 1))
                        pe.nop().then_inc(a_read[n], 1)
                    if m == 1:
                        wait_for_up(n, c, q)
                        lora_up(n, 0)
                    if m >= 1:
                        lora_up(n, m)

            def base_slice(k):
                for i, (part_of_w, part_of_x) in enumerate(PASSES):
                    if (part_of_w, part_of_x) == (HI, HI):
                        pe.wait_ge(w_hi[0], k + 1)
                        pe.wait_ge(x_hi[0], k + 1)
                    elif part_of_x == LO:
                        pe.wait_ge(x_lo[0], k + 1)
                    else:
                        pe.wait_ge(w_lo[0], k + 1)
                    for m in range(SLICES):
                        last = base(0, m, k, part_of_w, part_of_x, k == 0 and i == 0)
                return last

            for k in range(SLICES - 1):
                base_slice(k)
            pe.wait_ge(a_lo[0], 1)
            for k in range(SLICES):
                if k == SLICES - 1:
                    pe.wait_ge(x_lo[0], SLICES)
                for g in range(GROUPS):
                    last = lora_down(0, g, k)
                    if k == SLICES - 1:
                        last.then_inc(h_ready, 1)
                if k < SLICES - 1:
                    last.then_inc(x_read[0], 1)
            pe.wait_ge(h_ready, GROUPS)
            pe.nop().then_inc(a_read[0], 1)
            base_slice(SLICES - 1).then_inc(x_read[0], 1)
            wait_for_up(0, 0, 0)
            for m in range(SLICES):
                lora_up(0, m)
            pe.wait_ge(w_lo[1], SLICES)
            with pe.Fori(0, CHUNKS - 1) as j:
                phase(0, j + 1, 2 * j + 1)
                phase(1, j, 2 * j + 2)
            phase(1, CHUNKS - 1, 2 * CHUNKS - 1)


def kernel(x, itok_B_6_15, itok_B_0_23, L0_cond_base_weight, L0_cond_base_bias, L0_cond_lora_A_w,
           L0_cond_lora_B_w, L1_cond_W, L1_cond_b, L1_cond_lora_As, L1_cond_lora_Bs):
    import numpy as np
    import concourse.bacc as bacc
    from concourse.bass_utils import run_bass_kernel_spmd

    def arr(a):
        return np.ascontiguousarray(np.asarray(a))

    def feature_slices(a):
        a = np.asarray(a)
        return arr(a.reshape(a.shape[:-1] + (P, SLICES)).swapaxes(-1, -2))

    ids = np.stack([np.asarray(itok_B_6_15), np.asarray(itok_B_0_23)])
    by_row = np.repeat(ids.reshape(LAYERS, CHUNKS * GROUPS, GROUP_BATCHES).transpose(2, 0, 1), RANK, axis=0)
    ins = {
        "in_xT": arr(np.asarray(x).reshape(TOKENS, FEATURES).T),
        "in_ids": arr(ids.reshape(1, LAYERS * BATCHES)),
        "in_ids_by_row": arr(by_row.reshape(P, LAYERS * CHUNKS * GROUPS)),
        "in_w0": feature_slices(np.asarray(L0_cond_base_weight).T),
        "in_w1": feature_slices(np.asarray(L1_cond_W).T),
        "in_bias": arr(np.concatenate([np.asarray(L0_cond_base_bias).reshape(P, SLICES),
                                       np.asarray(L1_cond_b).reshape(P, SLICES)], axis=1)),
        "in_a0": arr(np.asarray(L0_cond_lora_A_w).transpose(0, 2, 1)).reshape(ADAPTERS, P, SLICES * RANK),
        "in_a1": arr(L1_cond_lora_As).reshape(ADAPTERS, P, SLICES * RANK),
        "in_b0": feature_slices(np.asarray(L0_cond_lora_B_w).transpose(0, 2, 1)).reshape(
            ADAPTERS * RANK, FEATURES),
        "in_b1": feature_slices(L1_cond_lora_Bs).reshape(ADAPTERS * RANK, FEATURES),
    }
    nc = bacc.Bacc("TRN2", target_bir_lowering=False, num_devices=1)
    t = {name: nc.dram_tensor(name, a.shape, mybir.dt.from_np(a.dtype), kind="ExternalInput").ap()
         for name, a in ins.items()}
    out = nc.dram_tensor("out_yT", (FEATURES, TOKENS), F32, kind="ExternalOutput").ap()
    lora_layers_kernel(nc, t["in_xT"], t["in_ids"], t["in_ids_by_row"], (t["in_w0"], t["in_w1"]),
                       t["in_bias"], (t["in_a0"], t["in_a1"]), (t["in_b0"], t["in_b1"]), out)
    r = run_bass_kernel_spmd(nc, [ins], core_ids=[0])
    return arr(r.results[0]["out_yT"].T).reshape(BATCHES, SEQ, FEATURES)
```

```python
from contextlib import ExitStack

import concourse.bass as bass
from concourse import mybir

F32 = mybir.dt.float32
F32R = mybir.dt.float32r
I32 = mybir.dt.int32
U32 = mybir.dt.uint32
ALU = mybir.AluOpType

P = 128
BATCHES, SEQ, FEATURES = 64, 32, 512
ADAPTERS, RANK = 32, 16
TOKENS = BATCHES * SEQ
SLICES = FEATURES // P
CHUNK = 512
CHUNKS = TOKENS // CHUNK
GROUP_BATCHES = P // RANK
GROUP = GROUP_BATCHES * SEQ
GROUPS = CHUNK // GROUP
CHUNK_BATCHES = CHUNK // SEQ
QUADS = 2
QUAD_BATCHES = GROUP_BATCHES // QUADS
QUAD_ROWS = QUAD_BATCHES * RANK
QUAD = QUAD_BATCHES * SEQ
CHUNK_QUADS = GROUPS * QUADS
LAYERS = 2
LORA_SCALE = (1.0, 2.0)
SP_SLICES, POOL_SLICES = (0, 1), (2, 3)
LORA_LAG = 2
H_STEPS = 4
DMA = 16
HI, LO = 0, 1
PASSES = ((HI, HI), (HI, LO), (LO, HI))


def lora_layers_kernel(nc, xT, ids, ids_by_row, w, bias, lora_a, lora_b, outT):
    with ExitStack() as ctx:
        def sb(name, shape, dt=F32):
            return ctx.enter_context(nc.sbuf_tensor(name, shape, dt))

        def psum(name, shape):
            return ctx.enter_context(nc.psum_tensor(name, shape, F32))

        def sem(name):
            return ctx.enter_context(nc.semaphore(name))

        def pair(make, name, *args):
            return [make(f"{name}{n}", *args) for n in range(2)]

        def parts(name, shape):
            return [[sb(f"{name}{n}_{part}", shape, F32R) for part in ("hi", "lo")] for n in range(2)]

        x = sb("x_all", [P, SLICES, TOKENS])
        x_parts = pair(sb, "x_parts", [P, 2, SLICES, CHUNK], F32R)
        w_raw = pair(sb, "w_raw", [P, SLICES, FEATURES])
        w_parts = parts("w", [P, SLICES, SLICES, P])
        bias_sb = sb("bias_sb", [P, LAYERS * SLICES])
        a_raw = pair(sb, "a_raw", [P, CHUNK_BATCHES, SLICES, RANK])
        a_parts = pair(sb, "a_parts", [P, SLICES, CHUNK_QUADS, 2, QUAD_ROWS], F32R)
        b_raw = pair(sb, "b_raw", [P, CHUNKS * GROUPS, FEATURES])
        b_parts = parts("b", [P, GROUPS, FEATURES])
        h_other = sb("h_other", [P, GROUPS, 2, QUAD])
        h_both = sb("h_both", [P, GROUPS, 2, QUAD])
        h_sum = sb("h_sum", [P, GROUPS, QUAD])
        h_masked = sb("h_masked", [P, GROUPS, QUAD])
        h_parts = [sb(f"h_{part}", [P, GROUPS, GROUP], F32R) for part in ("hi", "lo")]
        own_in_group = sb("own_in_group", [P, GROUP_BATCHES, SEQ])
        own_batch = sb("own_batch", [P, QUAD_BATCHES, SEQ])
        ids_sb = sb("ids_sb", [1, LAYERS * BATCHES], I32)
        ids_row_sb = sb("ids_row_sb", [P, LAYERS * CHUNKS * GROUPS], I32)
        partition = sb("partition", [P, 1], I32)
        rank_row = sb("rank_row", [P, 1], I32)
        rank_row_f = sb("rank_row_f", [P, 1])
        b_index = sb("b_index", [P, LAYERS * CHUNKS * GROUPS], U32)

        out_bank = [psum(f"out_bank{m}", [P, CHUNK]) for m in range(SLICES)]
        h_bank = [psum(f"h_bank{g}", [P, QUADS, 2, QUAD]) for g in range(GROUPS)]

        ids_landed = sem("ids_landed")
        ids_row_landed = sem("ids_row_landed")
        bias_landed = sem("bias_landed")
        w0_landed = [sem(f"w0_landed{k}") for k in range(SLICES)]
        w1_landed = sem("w1_landed")
        x0_landed = [sem(f"x0_landed{k}") for k in range(SLICES)]
        x1_landed = sem("x_chunk1_landed")
        x_rest_landed = sem("x_rest_landed")
        a_landed = pair(sem, "a_landed")
        b_landed = [sem(f"b_landed_phase{q}") for q in range(3)]
        b_rest_landed = sem("b_rest_landed")
        stored = sem("stored")
        index_steps = sem("index_steps")
        mask_steps = sem("mask_steps")
        w_hi = pair(sem, "w_hi")
        w_lo = pair(sem, "w_lo")
        x_hi = pair(sem, "x_hi")
        x_lo = pair(sem, "x_lo")
        a_hi = pair(sem, "a_hi")
        a_lo = pair(sem, "a_lo")
        b_hi = pair(sem, "b_hi")
        b_lo = pair(sem, "b_lo")
        h_moved = sem("h_moved")
        h_steps = sem("h_steps")
        h_hi = sem("h_hi")
        h_lo = sem("h_lo")
        h_zero = sem("h_zero")
        bank_evicted = sem("bank_evicted")
        h_ready = sem("h_ready")
        bank_ready = sem("bank_ready")

        xT_v = xT.rearrange("(p k) t -> p k t", k=SLICES)
        outT_v = outT.rearrange("(p k) t -> p k t", k=SLICES)
        w_v = [v.rearrange("(p k) m q -> p k (m q)", k=SLICES) for v in w]

        def chunk_of(c):
            return bass.ds(c * CHUNK, CHUNK)

        def f32(ap):
            return ap.bitcast(F32)

        def a_part(s, part):
            return a_parts[s][:, :, :, part, :]

        def a_quads(s):
            return a_raw[s][:].rearrange("p b k r -> p k b r")

        def quad_rows(u):
            return slice(u * QUAD_ROWS, (u + 1) * QUAD_ROWS)

        block = ctx.enter_context(nc.Block())

        @block.sync
        def _(sp):
            for k in SP_SLICES:
                sp.dma_start(w_raw[0][:, k, :], w_v[0][:, k, :]).then_inc(w0_landed[k], DMA)
                sp.dma_start(x[:, k, 0:CHUNK], xT_v[:, k, 0:CHUNK]).then_inc(x0_landed[k], DMA)
                if k == 0:
                    sp.dma_start(ids_sb[:], ids).then_inc(ids_landed, DMA)
            sp.wait_ge(ids_landed, DMA)
            id_regs = [sp.alloc_register(f"adapter_id{b}") for b in range(CHUNK_BATCHES)]

            def gather_a(s, n, c):
                sp.load(id_regs, ids_sb[0:1, bass.ds(n * BATCHES + c * CHUNK_BATCHES, CHUNK_BATCHES)])
                for b in range(CHUNK_BATCHES):
                    adapter = sp.snap(id_regs[b], min_val=0, max_val=ADAPTERS - 1)
                    sp.dma_start(a_raw[s][:, b, :, :].rearrange("p k r -> p (k r)"),
                                 lora_a[n][bass.ds(adapter, 1)].rearrange("a p e -> (a p) e")
                                 ).then_inc(a_landed[s], DMA)

            gather_a(0, 0, 0)
            gather_a(1, 0, 1)
            with sp.Fori(0, CHUNKS - 2) as j:
                sp.wait_ge(a_lo[0], j + 1)
                gather_a(0, 1, j)
                sp.wait_ge(a_lo[1], j + 1)
                gather_a(1, 0, j + 2)
            sp.wait_ge(a_lo[0], CHUNKS - 1)
            gather_a(0, 1, CHUNKS - 2)
            sp.wait_ge(a_lo[1], CHUNKS - 1)
            gather_a(1, 1, CHUNKS - 1)

        @block.gpsimd
        def _(pool):
            pool.iota(partition[:], pattern=[[0, 1]], base=0, channel_multiplier=1).then_inc(index_steps, 1)
            pool.dma_start(ids_row_sb[:], ids_by_row).then_inc(ids_row_landed, DMA)
            pool.memset(own_in_group[:], 1.0).then_inc(mask_steps, 1)
            for k in POOL_SLICES:
                pool.dma_start(w_raw[0][:, k, :], w_v[0][:, k, :]).then_inc(w0_landed[k], DMA)
                pool.dma_start(x[:, k, 0:CHUNK], xT_v[:, k, 0:CHUNK]).then_inc(x0_landed[k], DMA)
            pool.wait_ge(index_steps, 4)

            def gather_b(n, g, landed):
                col = n * CHUNKS * GROUPS + g
                pool.indirect_dma_start(
                    out=b_raw[n][:, g, :], out_offset=None, in_=lora_b[n],
                    in_offset=bass.IndirectOffsetOnAxis(ap=b_index[:, col:col + 1], axis=0),
                ).then_inc(landed, DMA)

            def load_chunk(c, landed):
                pool.dma_start(x[:, :, c * CHUNK:(c + 1) * CHUNK],
                               xT_v[:, :, c * CHUNK:(c + 1) * CHUNK]).then_inc(landed, DMA)

            for g in range(GROUPS):
                gather_b(0, g, b_landed[0])
            pool.wait_ge(mask_steps, 1)
            pool.affine_select(out=own_in_group[:], in_=own_in_group[:], compare_op=ALU.is_ge, fill=0.0,
                               base=0, pattern=[[-RANK, GROUP_BATCHES], [0, SEQ]],
                               channel_multiplier=1).then_inc(mask_steps, 1)
            pool.wait_ge(mask_steps, 2)
            pool.affine_select(out=own_in_group[:], in_=own_in_group[:], compare_op=ALU.is_ge, fill=0.0,
                               base=RANK - 1, pattern=[[RANK, GROUP_BATCHES], [0, SEQ]],
                               channel_multiplier=-1).then_inc(mask_steps, 1)
            pool.dma_start(bias_sb[:], bias).then_inc(bias_landed, DMA)
            pool.wait_ge(x0_landed[SLICES - 1], DMA)
            load_chunk(1, x1_landed)
            for g in range(GROUPS, 2 * GROUPS):
                gather_b(0, g, b_landed[1])
            pool.wait_ge(a_landed[0], DMA * CHUNK_BATCHES)
            pool.dma_start(w_raw[1][:], w_v[1]).then_inc(w1_landed, DMA)
            for g in range(GROUPS):
                gather_b(1, g, b_landed[2])

            def b_low(s, n, c, phases_of_set):
                pool.wait_ge(b_hi[s], phases_of_set + 1)
                pool.tensor_tensor(b_parts[s][LO][:], b_raw[n][:, bass.ds(c * GROUPS, GROUPS), :],
                                   f32(b_parts[s][HI][:]), ALU.subtract).then_inc(b_lo[s], 1)

            def low_parts(s, n, c, phases_of_set):
                pool.wait_ge(a_hi[s], phases_of_set + 1)
                pool.tensor_tensor(a_part(s, LO), a_quads(s), f32(a_part(s, HI)), ALU.subtract
                                   ).then_inc(a_lo[s], 1)
                b_low(s, n, c, phases_of_set)

            b_low(1, 0, 1, 0)
            for c in range(2, CHUNKS):
                load_chunk(c, x_rest_landed)
                for g in range(c * GROUPS, (c + 1) * GROUPS):
                    gather_b(0, g, b_rest_landed)
            for g in range(GROUPS, CHUNKS * GROUPS):
                gather_b(1, g, b_rest_landed)
            with pool.Fori(0, CHUNKS - 2) as j:
                low_parts(0, 1, j, j + 1)
                low_parts(1, 0, j + 2, j + 1)
            low_parts(0, 1, CHUNKS - 2, CHUNKS - 1)
            low_parts(1, 1, CHUNKS - 1, CHUNKS - 1)

        @block.scalar
        def _(act):
            act.wait_ge(index_steps, 2)
            nc.scalar.copy(rank_row_f[:], rank_row[:]).then_inc(index_steps, 1)

            def x_high(s, c, k):
                nc.scalar.copy(x_parts[s][:, HI, k, :], x[:, k, chunk_of(c)]).then_inc(x_hi[s], 1)

            def a_high(s):
                nc.scalar.copy(a_part(s, HI), a_quads(s)).then_inc(a_hi[s], 1)

            def b_high(s, n, c):
                nc.scalar.copy(b_parts[s][HI][:], b_raw[n][:, bass.ds(c * GROUPS, GROUPS), :]
                               ).then_inc(b_hi[s], 1)

            def h_move(q):
                for g in range(GROUPS):
                    act.wait_ge(h_ready, GROUPS * q + g + 1)
                    for u in range(QUADS):
                        nc.scalar.copy(h_other[quad_rows(u), g, :, :],
                                       h_bank[g][quad_rows(1 - u), u, :, :]).then_inc(h_moved, 1)

            def h_high(q):
                for g in range(GROUPS):
                    act.wait_ge(h_steps, H_STEPS * (GROUPS * q + g + 1))
                    for u in range(QUADS):
                        nc.scalar.copy(h_parts[HI][quad_rows(u), g, u * QUAD:(u + 1) * QUAD],
                                       h_masked[quad_rows(u), g, :]).then_inc(h_hi, 1)

            def phase(s, n, c, q, phases_of_set):
                act.wait_ge(bank_ready, SLICES * (q - 1))
                for k in range(SLICES):
                    x_high(s, c, k)
                h_move(q - 1)
                act.wait_ge(a_landed[s], DMA * CHUNK_BATCHES * (phases_of_set + 1))
                a_high(s)
                b_high(s, n, c)
                h_high(q - 1)

            def store(c, q):
                for m in range(SLICES):
                    act.wait_ge(bank_evicted, SLICES * q + m + 1)
                    act.dma_start(outT_v[:, m, chunk_of(c)], x[:, m, chunk_of(c)]).then_inc(stored, DMA)

            for k in range(SLICES):
                act.wait_ge(x0_landed[k], DMA)
                x_high(0, 0, k)
            act.wait_ge(b_landed[0], DMA * GROUPS)
            b_high(0, 0, 0)
            act.wait_ge(a_landed[0], DMA * CHUNK_BATCHES)
            a_high(0)
            act.wait_ge(x1_landed, DMA)
            for k in range(SLICES):
                x_high(1, 1, k)
            h_move(0)
            h_high(0)
            act.wait_ge(b_landed[1], DMA * GROUPS)
            b_high(1, 0, 1)
            act.wait_ge(a_landed[1], DMA * CHUNK_BATCHES)
            a_high(1)
            act.wait_ge(w1_landed, DMA)
            for k in range(SLICES):
                nc.scalar.copy(w_parts[1][HI][:, k, :, :], w_raw[1][:, k, :]).then_inc(w_hi[1], 1)
            act.wait_ge(b_landed[2], DMA * GROUPS)

            def phase_l1(j):
                act.wait_ge(bank_evicted, SLICES * (2 * j + 1))
                phase(0, 1, j, 2 * j + 2, j + 1)

            phase_l1(0)
            act.wait_ge(x_rest_landed, DMA * (CHUNKS - 2))
            act.wait_ge(b_rest_landed, DMA * GROUPS * (LAYERS * CHUNKS - 3))
            with act.Fori(0, CHUNKS - 2) as j:
                phase(1, 0, j + 2, 2 * j + 3, j + 1)
                store(j, 2 * j + 2)
                phase_l1(j + 1)
            act.wait_ge(bank_evicted, SLICES * (2 * CHUNKS - 2))
            phase(1, 1, CHUNKS - 1, 2 * CHUNKS - 1, CHUNKS - 1)
            store(CHUNKS - 2, 2 * CHUNKS - 2)
            h_move(2 * CHUNKS - 1)
            h_high(2 * CHUNKS - 1)
            store(CHUNKS - 1, 2 * CHUNKS - 1)
            act.wait_ge(stored, DMA * SLICES * CHUNKS)

        @block.vector
        def _(dve):
            for part in (HI, LO):
                dve.memset(f32(h_parts[part][:]), 0.0).then_inc(h_zero, 1)
            dve.wait_ge(index_steps, 1)
            dve.tensor_scalar(rank_row[:], partition[:], RANK - 1, None, ALU.bitwise_and
                              ).then_inc(index_steps, 1)
            dve.wait_ge(index_steps, 3)
            dve.wait_ge(ids_row_landed, DMA)
            dve.tensor_scalar(b_index[:], ids_row_sb[:], float(RANK), rank_row_f[:, 0:1], ALU.mult, ALU.add
                              ).then_inc(index_steps, 1)

            def w_low(n, k):
                dve.wait_ge(w_hi[n], k + 1)
                dve.tensor_tensor(w_parts[n][LO][:, k, :, :].rearrange("p m q -> p (m q)"),
                                  w_raw[n][:, k, :],
                                  f32(w_parts[n][HI][:, k, :, :]).rearrange("p m q -> p (m q)"),
                                  ALU.subtract).then_inc(w_lo[n], 1)

            def x_low(s, c, phases_of_set):
                for k in range(SLICES):
                    dve.wait_ge(x_hi[s], SLICES * phases_of_set + k + 1)
                    dve.tensor_tensor(x_parts[s][:, LO, k, :], x[:, k, chunk_of(c)],
                                      f32(x_parts[s][:, HI, k, :]), ALU.subtract).then_inc(x_lo[s], 1)

            def mask_and_low(n, q):
                for g in range(GROUPS):
                    before = H_STEPS * (GROUPS * q + g)
                    dve.wait_ge(h_moved, QUADS * (GROUPS * q + g + 1))
                    for u in range(QUADS):
                        dve.tensor_tensor(h_both[quad_rows(u), g, :, :], h_bank[g][quad_rows(u), u, :, :],
                                          h_other[quad_rows(u), g, :, :], ALU.add).then_inc(h_steps, 1)
                    dve.wait_ge(h_steps, before + 2)
                    dve.tensor_tensor(h_sum[:, g, :], h_both[:, g, HI, :], h_both[:, g, LO, :], ALU.add
                                      ).then_inc(h_steps, 1)
                    dve.wait_ge(h_steps, before + 3)
                    dve.scalar_tensor_tensor(
                        out=h_masked[:, g, :], in0=h_sum[:, g, :], scalar=LORA_SCALE[n],
                        in1=own_batch[:].rearrange("p b s -> p (b s)"), op0=ALU.mult, op1=ALU.mult,
                    ).then_inc(h_steps, 1)
                for g in range(GROUPS):
                    for u in range(QUADS):
                        dve.wait_ge(h_hi, QUADS * (GROUPS * q + g) + u + 1)
                        block_of = (quad_rows(u), g, slice(u * QUAD, (u + 1) * QUAD))
                        dve.tensor_tensor(h_parts[LO][block_of], h_masked[quad_rows(u), g, :],
                                          f32(h_parts[HI][block_of]), ALU.subtract).then_inc(h_lo, 1)

            def evict(n, c, q):
                for m in range(SLICES):
                    dve.wait_ge(bank_ready, SLICES * q + m + 1)
                    col = n * SLICES + m
                    dve.scalar_tensor_tensor(
                        out=x[:, m, chunk_of(c)], in0=out_bank[m][:], scalar=bias_sb[:, col:col + 1],
                        in1=x[:, m, chunk_of(c)], op0=ALU.add, op1=ALU.add).then_inc(bank_evicted, 1)

            for k in range(SLICES):
                dve.wait_ge(w0_landed[k], DMA)
                dve.tensor_copy(w_parts[0][HI][:, k, :, :].rearrange("p m q -> p (m q)"), w_raw[0][:, k, :]
                                ).then_inc(w_hi[0], 1)
                w_low(0, k)
                dve.wait_ge(x_hi[0], k + 1)
                dve.tensor_tensor(x_parts[0][:, LO, k, :], x[:, k, 0:CHUNK],
                                  f32(x_parts[0][:, HI, k, :]), ALU.subtract).then_inc(x_lo[0], 1)
            dve.wait_ge(b_hi[0], 1)
            dve.tensor_tensor(b_parts[0][LO][:], b_raw[0][:, 0:GROUPS, :], f32(b_parts[0][HI][:]),
                              ALU.subtract).then_inc(b_lo[0], 1)
            dve.wait_ge(a_hi[0], 1)
            dve.tensor_tensor(a_part(0, LO), a_quads(0), f32(a_part(0, HI)), ALU.subtract
                              ).then_inc(a_lo[0], 1)
            dve.wait_ge(mask_steps, 3)
            dve.tensor_tensor(own_batch[:], own_in_group[:, 0:QUAD_BATCHES, :],
                              own_in_group[:, QUAD_BATCHES:, :], ALU.add).then_inc(mask_steps, 1)
            dve.wait_ge(mask_steps, 4)
            dve.wait_ge(bias_landed, DMA)
            x_low(1, 1, 0)
            mask_and_low(0, 0)
            dve.wait_ge(a_hi[1], 1)
            dve.tensor_tensor(a_part(1, LO), a_quads(1), f32(a_part(1, HI)), ALU.subtract
                              ).then_inc(a_lo[1], 1)
            evict(0, 0, 0)
            for k in range(SLICES):
                w_low(1, k)
            x_low(0, 0, 1)
            mask_and_low(0, 1)
            evict(0, 1, 1)
            with dve.Fori(0, CHUNKS - 2) as j:
                x_low(1, j + 2, j + 1)
                mask_and_low(1, 2 * j + 2)
                evict(1, j, 2 * j + 2)
                x_low(0, j + 1, j + 2)
                mask_and_low(0, 2 * j + 3)
                evict(0, j + 2, 2 * j + 3)
            x_low(1, CHUNKS - 1, CHUNKS - 1)
            mask_and_low(1, 2 * CHUNKS - 2)
            evict(1, CHUNKS - 2, 2 * CHUNKS - 2)
            mask_and_low(1, 2 * CHUNKS - 1)
            evict(1, CHUNKS - 1, 2 * CHUNKS - 1)

        @block.tensor
        def _(pe):
            def base(s, n, m, k, part_of_w, part_of_x, first):
                return nc.tensor.matmul(out_bank[m][:], w_parts[n][part_of_w][:, k, m, :],
                                        x_parts[s][:, part_of_x, k, :], start=first, stop=False)

            def lora_down(s, g):
                for u in range(QUADS):
                    quad = g * QUADS + u
                    for k in range(SLICES):
                        last = nc.tensor.matmul(
                            h_bank[g][:, u, :, :], a_parts[s][:, k, quad, :, :].rearrange("p a c -> p (a c)"),
                            x_parts[s][:, :, k, quad * QUAD:(quad + 1) * QUAD],
                            start=(k == 0), stop=(k == SLICES - 1))
                last.then_inc(h_ready, 1)

            def lora_up(s, m, g):
                for i, (part_of_b, part_of_h) in enumerate(PASSES):
                    last = nc.tensor.matmul(
                        out_bank[m][:, g * GROUP:(g + 1) * GROUP],
                        b_parts[s][part_of_b][:, g, m * P:(m + 1) * P], h_parts[part_of_h][:, g, :],
                        start=False, stop=(g == GROUPS - 1 and i == len(PASSES) - 1))
                return last

            def finish_bank(s, m):
                for g in range(GROUPS):
                    last = lora_up(s, m, g)
                last.then_inc(bank_ready, 1)

            def phase(s, n, q, phases_of_set):
                pe.wait_ge(x_lo[s], SLICES * (phases_of_set + 1))
                for m in range(SLICES):
                    pe.wait_ge(bank_evicted, SLICES * (q - 1) + m + 1)
                    for k in range(SLICES):
                        for i, (part_of_w, part_of_x) in enumerate(PASSES):
                            base(s, n, m, k, part_of_w, part_of_x, k == 0 and i == 0)
                    if m == 0:
                        pe.wait_ge(a_lo[s], phases_of_set + 1)
                        pe.wait_ge(h_steps, H_STEPS * GROUPS * q)
                        for g in range(GROUPS):
                            lora_down(s, g)
                    if m == LORA_LAG:
                        pe.wait_ge(b_lo[s], phases_of_set + 1)
                        pe.wait_ge(h_lo, QUADS * GROUPS * (q + 1))
                        for done in range(m):
                            finish_bank(s, done)
                    if m >= LORA_LAG:
                        finish_bank(s, m)

            for k in range(SLICES):
                pe.wait_ge(w_hi[0], k + 1)
                pe.wait_ge(x_hi[0], k + 1)
                for m in range(SLICES):
                    base(0, 0, m, k, HI, HI, k == 0)
                if k == SLICES - 1:
                    break
                pe.wait_ge(w_lo[0], k + 1)
                for m in range(SLICES):
                    base(0, 0, m, k, LO, HI, False)
                pe.wait_ge(x_lo[0], k + 1)
                for m in range(SLICES):
                    base(0, 0, m, k, HI, LO, False)
            pe.wait_ge(x_lo[0], SLICES)
            pe.wait_ge(a_lo[0], 1)
            for g in range(GROUPS):
                lora_down(0, g)
            pe.wait_ge(w_lo[0], SLICES)
            for part_of_w, part_of_x in PASSES[1:]:
                for m in range(SLICES):
                    base(0, 0, m, SLICES - 1, part_of_w, part_of_x, False)
            pe.wait_ge(b_lo[0], 1)
            for g in range(GROUPS):
                pe.wait_ge(h_lo, QUADS * (g + 1))
                for m in range(SLICES):
                    last = lora_up(0, m, g)
                    if g == GROUPS - 1:
                        last.then_inc(bank_ready, 1)
            with pe.Fori(0, CHUNKS - 1) as j:
                phase(1, 0, 2 * j + 1, j)
                pe.wait_ge(w_lo[1], SLICES)
                phase(0, 1, 2 * j + 2, j + 1)
            phase(1, 1, 2 * CHUNKS - 1, CHUNKS - 1)


def kernel(x, itok_B_6_15, itok_B_0_23, L0_cond_base_weight, L0_cond_base_bias, L0_cond_lora_A_w,
           L0_cond_lora_B_w, L1_cond_W, L1_cond_b, L1_cond_lora_As, L1_cond_lora_Bs):
    import numpy as np
    import concourse.bacc as bacc
    from concourse.bass_utils import run_bass_kernel_spmd

    def arr(a):
        return np.ascontiguousarray(np.asarray(a))

    def feature_slices(a):
        a = np.asarray(a)
        return arr(a.reshape(a.shape[:-1] + (P, SLICES)).swapaxes(-1, -2))

    ids = np.stack([np.asarray(itok_B_6_15), np.asarray(itok_B_0_23)])
    by_row = np.repeat(ids.reshape(LAYERS, CHUNKS * GROUPS, GROUP_BATCHES).transpose(2, 0, 1), RANK, axis=0)
    ins = {
        "in_xT": arr(np.asarray(x).reshape(TOKENS, FEATURES).T),
        "in_ids": arr(ids.reshape(1, LAYERS * BATCHES)),
        "in_ids_by_row": arr(by_row.reshape(P, LAYERS * CHUNKS * GROUPS)),
        "in_w0": feature_slices(np.asarray(L0_cond_base_weight).T),
        "in_w1": feature_slices(np.asarray(L1_cond_W).T),
        "in_bias": arr(np.concatenate([np.asarray(L0_cond_base_bias).reshape(P, SLICES),
                                       np.asarray(L1_cond_b).reshape(P, SLICES)], axis=1)),
        "in_a0": arr(np.asarray(L0_cond_lora_A_w).transpose(0, 2, 1)).reshape(ADAPTERS, P, SLICES * RANK),
        "in_a1": arr(L1_cond_lora_As).reshape(ADAPTERS, P, SLICES * RANK),
        "in_b0": feature_slices(np.asarray(L0_cond_lora_B_w).transpose(0, 2, 1)).reshape(
            ADAPTERS * RANK, FEATURES),
        "in_b1": feature_slices(L1_cond_lora_Bs).reshape(ADAPTERS * RANK, FEATURES),
    }
    nc = bacc.Bacc("TRN2", target_bir_lowering=False, num_devices=1)
    t = {name: nc.dram_tensor(name, a.shape, mybir.dt.from_np(a.dtype), kind="ExternalInput").ap()
         for name, a in ins.items()}
    out = nc.dram_tensor("out_yT", (FEATURES, TOKENS), F32, kind="ExternalOutput").ap()
    lora_layers_kernel(nc, t["in_xT"], t["in_ids"], t["in_ids_by_row"], (t["in_w0"], t["in_w1"]),
                       t["in_bias"], (t["in_a0"], t["in_a1"]), (t["in_b0"], t["in_b1"]), out)
    r = run_bass_kernel_spmd(nc, [ins], core_ids=[0])
    return arr(r.results[0]["out_yT"].T).reshape(BATCHES, SEQ, FEATURES)
```

```python
from contextlib import ExitStack

import concourse.bass as bass
from concourse import mybir

F32 = mybir.dt.float32
F32R = mybir.dt.float32r
I32 = mybir.dt.int32
U32 = mybir.dt.uint32
ALU = mybir.AluOpType

P = 128
BATCHES, SEQ, FEATURES = 64, 32, 512
ADAPTERS, RANK = 32, 16
TOKENS = BATCHES * SEQ
SLICES = FEATURES // P
CHUNK = 512
CHUNKS = TOKENS // CHUNK
GROUP_BATCHES = P // RANK
GROUP = GROUP_BATCHES * SEQ
GROUPS = CHUNK // GROUP
CHUNK_BATCHES = CHUNK // SEQ
QUADS = 2
QUAD_BATCHES = GROUP_BATCHES // QUADS
QUAD_ROWS = QUAD_BATCHES * RANK
QUAD = QUAD_BATCHES * SEQ
CHUNK_QUADS = GROUPS * QUADS
LAYERS = 2
LORA_SCALE = (1.0, 2.0)
SP_SLICES, POOL_SLICES = (0, 1), (2, 3)
LORA_LAG = 2
EARLY = 2
FIRST_ORDER = (*range(EARLY, SLICES), *range(EARLY))
W1_EARLY = 2
WARM_UP = 17
H_STEPS = 4
DMA = 16
HI, LO = 0, 1
PASSES = ((HI, HI), (HI, LO), (LO, HI))


def lora_layers_kernel(nc, xT, ids, ids_by_row, w, bias, lora_a, lora_b, outT):
    with ExitStack() as ctx:
        def sb(name, shape, dt=F32):
            return ctx.enter_context(nc.sbuf_tensor(name, shape, dt))

        def psum(name, shape):
            return ctx.enter_context(nc.psum_tensor(name, shape, F32))

        def sem(name):
            return ctx.enter_context(nc.semaphore(name))

        def pair(make, name, *args):
            return [make(f"{name}{n}", *args) for n in range(2)]

        def parts(name, shape):
            return [[sb(f"{name}{n}_{part}", shape, F32R) for part in ("hi", "lo")] for n in range(2)]

        x = sb("x_all", [P, SLICES, TOKENS])
        x_parts = pair(sb, "x_parts", [P, 2, SLICES, CHUNK], F32R)
        w_raw = pair(sb, "w_raw", [P, SLICES, FEATURES])
        w_parts = parts("w", [P, SLICES, SLICES, P])
        bias_sb = sb("bias_sb", [P, LAYERS * SLICES])
        a_raw = pair(sb, "a_raw", [P, CHUNK_BATCHES, SLICES, RANK])
        a_parts = pair(sb, "a_parts", [P, SLICES, CHUNK_QUADS, 2, QUAD_ROWS], F32R)
        b_raw = pair(sb, "b_raw", [P, CHUNKS * GROUPS, FEATURES])
        b_parts = parts("b", [P, GROUPS, FEATURES])
        h_other = sb("h_other", [P, GROUPS, 2, QUAD])
        h_both = sb("h_both", [P, GROUPS, 2, QUAD])
        h_sum = sb("h_sum", [P, GROUPS, QUAD])
        h_masked = sb("h_masked", [P, GROUPS, QUAD])
        h_parts = [sb(f"h_{part}", [P, GROUPS, GROUP], F32R) for part in ("hi", "lo")]
        own_in_group = sb("own_in_group", [P, GROUP_BATCHES, SEQ])
        own_batch = sb("own_batch", [P, QUAD_BATCHES, SEQ])
        ids_sb = sb("ids_sb", [1, LAYERS * BATCHES], I32)
        ids_row_sb = sb("ids_row_sb", [P, LAYERS * CHUNKS * GROUPS], I32)
        partition = sb("partition", [P, 1], I32)
        rank_row = sb("rank_row", [P, 1], I32)
        rank_row_f = sb("rank_row_f", [P, 1])
        b_index = sb("b_index", [P, LAYERS * CHUNKS * GROUPS], U32)

        out_bank = [psum(f"out_bank{m}", [P, CHUNK]) for m in range(SLICES)]
        first_bank = [psum(f"first_bank{m}", [P, CHUNK]) for m in range(EARLY)] + out_bank[EARLY:]
        last_bank = [out_bank[SLICES - 1], first_bank[0]]
        h_bank = [psum(f"h_bank{g}", [P, QUADS, 2, QUAD]) for g in range(GROUPS)]

        ids_landed = sem("ids_landed")
        ids_row_landed = sem("ids_row_landed")
        bias_landed = sem("bias_landed")
        w0_landed = [sem(f"w0_landed{k}") for k in range(SLICES)]
        w1_landed = sem("w1_landed")
        x0_landed = [sem(f"x0_landed{k}") for k in range(SLICES)]
        x_chunk1_landed = sem("x_chunk1_landed")
        x_rest_landed = sem("x_rest_landed")
        a_landed = [[sem(f"a_landed{s}_group{g}") for g in range(GROUPS)] for s in range(2)]
        b_landed = [sem(f"b_landed_phase{q}") for q in range(3)]
        b_rest_landed = pair(sem, "b_rest_landed")
        stored = sem("stored")
        index_steps = sem("index_steps")
        mask_steps = sem("mask_steps")
        w_hi = pair(sem, "w_hi")
        w_lo = pair(sem, "w_lo")
        x_hi = pair(sem, "x_hi")
        x_lo = pair(sem, "x_lo")
        a_hi = pair(sem, "a_hi")
        a_lo = pair(sem, "a_lo")
        b_hi = pair(sem, "b_hi")
        b_lo = pair(sem, "b_lo")
        h_moved = sem("h_moved")
        h_steps = sem("h_steps")
        h_hi = sem("h_hi")
        h_lo = sem("h_lo")
        h_zero = sem("h_zero")
        bank_evicted = sem("bank_evicted")
        h_ready = sem("h_ready")
        bank_ready = sem("bank_ready")

        xT_v = xT.rearrange("(p k) t -> p k t", k=SLICES)
        outT_v = outT.rearrange("(p k) t -> p k t", k=SLICES)
        w_v = [v.rearrange("(p k) m q -> p k (m q)", k=SLICES) for v in w]

        def chunk_of(c):
            return bass.ds(c * CHUNK, CHUNK)

        def group_of_last_chunk(g):
            return slice((CHUNKS - 1) * CHUNK + g * GROUP, (CHUNKS - 1) * CHUNK + (g + 1) * GROUP)

        def f32(ap):
            return ap.bitcast(F32)

        def a_part(s, part, g):
            return a_parts[s][:, :, g * QUADS:(g + 1) * QUADS, part, :]

        def a_whole(s, g):
            return a_raw[s][:, g * GROUP_BATCHES:(g + 1) * GROUP_BATCHES].rearrange("p b k r -> p k b r")

        def quad_rows(u):
            return slice(u * QUAD_ROWS, (u + 1) * QUAD_ROWS)

        def split_w_low(engine, n, k):
            engine.wait_ge(w_hi[n], k + 1)
            engine.tensor_tensor(w_parts[n][LO][:, k, :, :].rearrange("p m q -> p (m q)"), w_raw[n][:, k, :],
                                 f32(w_parts[n][HI][:, k, :, :]).rearrange("p m q -> p (m q)"),
                                 ALU.subtract).then_inc(w_lo[n], 1)

        block = ctx.enter_context(nc.Block())

        @block.sync
        def _(sp):
            for k in SP_SLICES:
                sp.dma_start(w_raw[0][:, k, :], w_v[0][:, k, :]).then_inc(w0_landed[k], DMA)
                sp.dma_start(x[:, k, 0:CHUNK], xT_v[:, k, 0:CHUNK]).then_inc(x0_landed[k], DMA)
                if k == 0:
                    sp.dma_start(ids_sb[:], ids).then_inc(ids_landed, DMA)
            sp.wait_ge(ids_landed, DMA)
            id_regs = [sp.alloc_register(f"adapter_id{b}") for b in range(CHUNK_BATCHES)]

            def gather_a(s, n, c):
                sp.load(id_regs, ids_sb[0:1, bass.ds(n * BATCHES + c * CHUNK_BATCHES, CHUNK_BATCHES)])
                for b in range(CHUNK_BATCHES):
                    adapter = sp.snap(id_regs[b], min_val=0, max_val=ADAPTERS - 1)
                    sp.dma_start(a_raw[s][:, b, :, :].rearrange("p k r -> p (k r)"),
                                 lora_a[n][bass.ds(adapter, 1)].rearrange("a p e -> (a p) e")
                                 ).then_inc(a_landed[s][b // GROUP_BATCHES], DMA)

            gather_a(0, 0, 0)
            gather_a(1, 0, 1)
            with sp.Fori(0, CHUNKS - 2) as j:
                sp.wait_ge(a_lo[0], GROUPS * (j + 1))
                gather_a(0, 1, j)
                sp.wait_ge(a_lo[1], GROUPS * (j + 1))
                gather_a(1, 0, j + 2)
            sp.wait_ge(a_lo[0], GROUPS * (CHUNKS - 1))
            gather_a(0, 1, CHUNKS - 2)
            sp.wait_ge(a_lo[1], GROUPS * (CHUNKS - 1))
            gather_a(1, 1, CHUNKS - 1)

        @block.gpsimd
        def _(pool):
            pool.iota(partition[:], pattern=[[0, 1]], base=0, channel_multiplier=1).then_inc(index_steps, 1)
            pool.dma_start(ids_row_sb[:], ids_by_row).then_inc(ids_row_landed, DMA)
            pool.memset(own_in_group[:], 1.0).then_inc(mask_steps, 1)
            for k in POOL_SLICES:
                pool.dma_start(w_raw[0][:, k, :], w_v[0][:, k, :]).then_inc(w0_landed[k], DMA)
                pool.dma_start(x[:, k, 0:CHUNK], xT_v[:, k, 0:CHUNK]).then_inc(x0_landed[k], DMA)

            def gather_b(n, g, landed):
                col = n * CHUNKS * GROUPS + g
                pool.indirect_dma_start(
                    out=b_raw[n][:, g, :], out_offset=None, in_=lora_b[n],
                    in_offset=bass.IndirectOffsetOnAxis(ap=b_index[:, col:col + 1], axis=0),
                ).then_inc(landed, DMA)

            def load_chunk(c, landed):
                pool.dma_start(x[:, :, c * CHUNK:(c + 1) * CHUNK],
                               xT_v[:, :, c * CHUNK:(c + 1) * CHUNK]).then_inc(landed, DMA)

            load_chunk(1, x_chunk1_landed)
            pool.wait_ge(index_steps, 4)
            for g in range(GROUPS):
                gather_b(0, g, b_landed[0])
            pool.wait_ge(mask_steps, 1)
            pool.affine_select(out=own_in_group[:], in_=own_in_group[:], compare_op=ALU.is_ge, fill=0.0,
                               base=0, pattern=[[-RANK, GROUP_BATCHES], [0, SEQ]],
                               channel_multiplier=1).then_inc(mask_steps, 1)
            pool.wait_ge(mask_steps, 2)
            pool.affine_select(out=own_in_group[:], in_=own_in_group[:], compare_op=ALU.is_ge, fill=0.0,
                               base=RANK - 1, pattern=[[RANK, GROUP_BATCHES], [0, SEQ]],
                               channel_multiplier=-1).then_inc(mask_steps, 1)
            pool.dma_start(bias_sb[:], bias).then_inc(bias_landed, DMA)
            for g in range(GROUPS, 2 * GROUPS):
                gather_b(0, g, b_landed[1])
            pool.wait_ge(a_landed[0][GROUPS - 1], DMA * GROUP_BATCHES)
            pool.dma_start(w_raw[1][:], w_v[1]).then_inc(w1_landed, DMA)
            for g in range(GROUPS):
                gather_b(1, g, b_landed[2])
            pool.wait_ge(a_landed[1][GROUPS - 1], DMA * GROUP_BATCHES)
            load_chunk(2, x_rest_landed)

            def b_low(s, n, c, phases_of_set):
                pool.wait_ge(b_hi[s], phases_of_set + 1)
                pool.tensor_tensor(b_parts[s][LO][:], b_raw[n][:, bass.ds(c * GROUPS, GROUPS), :],
                                   f32(b_parts[s][HI][:]), ALU.subtract).then_inc(b_lo[s], 1)

            def low_parts(s, n, c, phases_of_set, groups=range(GROUPS)):
                for g in groups:
                    pool.wait_ge(a_hi[s], GROUPS * phases_of_set + g + 1)
                    pool.tensor_tensor(a_part(s, LO, g), a_whole(s, g), f32(a_part(s, HI, g)), ALU.subtract
                                       ).then_inc(a_lo[s], 1)
                b_low(s, n, c, phases_of_set)

            b_low(1, 0, 1, 0)
            for k in range(W1_EARLY):
                split_w_low(pool, 1, k)
            for c in range(2, CHUNKS):
                if c > 2:
                    load_chunk(c, x_rest_landed)
                for g in range(c * GROUPS, (c + 1) * GROUPS):
                    gather_b(0, g, b_rest_landed[0])
            low_parts(0, 1, 0, 1, range(GROUPS - 1))
            for g in range(GROUPS, CHUNKS * GROUPS):
                gather_b(1, g, b_rest_landed[1])
            with pool.Fori(0, CHUNKS - 2) as j:
                low_parts(1, 0, j + 2, j + 1)
                low_parts(0, 1, j + 1, j + 2)
            low_parts(1, 1, CHUNKS - 1, CHUNKS - 1)

        @block.scalar
        def _(act):
            act.wait_ge(index_steps, 2)
            nc.scalar.copy(rank_row_f[:], rank_row[:]).then_inc(index_steps, 1)

            def x_high(s, c, k):
                nc.scalar.copy(x_parts[s][:, HI, k, :], x[:, k, chunk_of(c)]).then_inc(x_hi[s], 1)

            def a_high(s, g):
                nc.scalar.copy(a_part(s, HI, g), a_whole(s, g)).then_inc(a_hi[s], 1)

            def set_a_high(s, phases_of_set):
                for g in range(GROUPS):
                    act.wait_ge(a_landed[s][g], DMA * GROUP_BATCHES * (phases_of_set + 1))
                    a_high(s, g)

            def b_high(s, n, c):
                nc.scalar.copy(b_parts[s][HI][:], b_raw[n][:, bass.ds(c * GROUPS, GROUPS), :]
                               ).then_inc(b_hi[s], 1)

            def h_move(q, groups=range(GROUPS)):
                for g in groups:
                    act.wait_ge(h_ready, GROUPS * q + g + 1)
                    for u in range(QUADS):
                        nc.scalar.copy(h_other[quad_rows(u), g, :, :],
                                       h_bank[g][quad_rows(1 - u), u, :, :]).then_inc(h_moved, 1)

            def h_high(q, groups=range(GROUPS)):
                for g in groups:
                    act.wait_ge(h_steps, H_STEPS * (GROUPS * q + g + 1))
                    for u in range(QUADS):
                        nc.scalar.copy(h_parts[HI][quad_rows(u), g, u * QUAD:(u + 1) * QUAD],
                                       h_masked[quad_rows(u), g, :]).then_inc(h_hi, 1)

            def phase(s, n, c, q, phases_of_set, b_source, gathers):
                h_move(q - 1)
                act.wait_ge(b_source, DMA * gathers)
                b_high(s, n, c)
                h_high(q - 1)
                for k in range(SLICES):
                    x_high(s, c, k)
                set_a_high(s, phases_of_set)

            def store(c, q):
                for m in range(SLICES):
                    act.wait_ge(bank_evicted, SLICES * q + m + 1)
                    act.dma_start(outT_v[:, m, chunk_of(c)], x[:, m, chunk_of(c)]).then_inc(stored, DMA)

            def store_last():
                for part in range(SLICES - 1 + GROUPS):
                    m = min(part, SLICES - 1)
                    tokens = chunk_of(CHUNKS - 1) if m < SLICES - 1 else group_of_last_chunk(part - m)
                    act.wait_ge(bank_evicted, SLICES * (2 * CHUNKS - 1) + part + 1)
                    act.dma_start(outT_v[:, m, tokens], x[:, m, tokens]).then_inc(stored, DMA)

            def w1_high(k):
                nc.scalar.copy(w_parts[1][HI][:, k, :, :], w_raw[1][:, k, :]).then_inc(w_hi[1], 1)

            for k in range(SLICES):
                act.wait_ge(x0_landed[k], DMA)
                x_high(0, 0, k)
            act.wait_ge(a_landed[0][0], DMA * GROUP_BATCHES)
            a_high(0, 0)
            act.wait_ge(x_chunk1_landed, DMA)
            for k in range(SLICES):
                x_high(1, 1, k)
            act.wait_ge(a_landed[0][1], DMA * GROUP_BATCHES)
            a_high(0, 1)
            h_move(0, [0])
            act.wait_ge(b_landed[0], DMA * GROUPS)
            b_high(0, 0, 0)
            h_high(0, [0])
            for g in range(1, GROUPS):
                h_move(0, [g])
                h_high(0, [g])
            act.wait_ge(a_landed[1][0], DMA * GROUP_BATCHES)
            a_high(1, 0)
            act.wait_ge(b_landed[1], DMA * GROUPS)
            b_high(1, 0, 1)
            act.wait_ge(w1_landed, DMA)
            for k in range(W1_EARLY):
                w1_high(k)
            act.wait_ge(a_landed[1][1], DMA * GROUP_BATCHES)
            a_high(1, 1)
            for k in range(W1_EARLY, SLICES):
                w1_high(k)

            rest_0 = (b_rest_landed[0], GROUPS * (CHUNKS - 2))
            rest_1 = (b_rest_landed[1], GROUPS * (CHUNKS - 1))
            h_move(1, [0])
            act.wait_ge(b_landed[2], DMA * GROUPS)
            b_high(0, 1, 0)
            h_high(1, [0])
            for g in range(1, GROUPS):
                h_move(1, [g])
                h_high(1, [g])
            act.wait_ge(bank_evicted, SLICES)
            for k in range(SLICES):
                x_high(0, 0, k)
            set_a_high(0, 1)
            act.wait_ge(x_rest_landed, DMA * (CHUNKS - 2))
            with act.Fori(0, CHUNKS - 2) as j:
                phase(1, 0, j + 2, 2 * j + 3, j + 1, *rest_0)
                store(j, 2 * j + 2)
                act.wait_ge(bank_evicted, SLICES * (2 * j + 3))
                phase(0, 1, j + 1, 2 * j + 4, j + 2, *rest_1)
            act.wait_ge(bank_evicted, SLICES * (2 * CHUNKS - 2))
            phase(1, 1, CHUNKS - 1, 2 * CHUNKS - 1, CHUNKS - 1, *rest_1)
            store(CHUNKS - 2, 2 * CHUNKS - 2)
            h_move(2 * CHUNKS - 1)
            h_high(2 * CHUNKS - 1)
            store_last()
            act.wait_ge(stored, DMA * (SLICES * CHUNKS + GROUPS - 1))

        @block.vector
        def _(dve):
            for part in (HI, LO):
                for g in range(GROUPS):
                    dve.memset(f32(h_parts[part][:, g, :]), 0.0).then_inc(h_zero, 1)
            dve.wait_ge(index_steps, 1)
            dve.tensor_scalar(rank_row[:], partition[:], RANK - 1, None, ALU.bitwise_and
                              ).then_inc(index_steps, 1)
            dve.wait_ge(index_steps, 3)
            dve.wait_ge(ids_row_landed, DMA)
            dve.tensor_scalar(b_index[:], ids_row_sb[:], float(RANK), rank_row_f[:, 0:1], ALU.mult, ALU.add
                              ).then_inc(index_steps, 1)

            def x_low(s, c, phases_of_set):
                for k in range(SLICES):
                    dve.wait_ge(x_hi[s], SLICES * phases_of_set + k + 1)
                    dve.tensor_tensor(x_parts[s][:, LO, k, :], x[:, k, chunk_of(c)],
                                      f32(x_parts[s][:, HI, k, :]), ALU.subtract).then_inc(x_lo[s], 1)

            def mask(n, q, g):
                before = H_STEPS * (GROUPS * q + g)
                dve.wait_ge(h_moved, QUADS * (GROUPS * q + g + 1))
                for u in range(QUADS):
                    dve.tensor_tensor(h_both[quad_rows(u), g, :, :], h_bank[g][quad_rows(u), u, :, :],
                                      h_other[quad_rows(u), g, :, :], ALU.add).then_inc(h_steps, 1)
                dve.wait_ge(h_steps, before + 2)
                dve.tensor_tensor(h_sum[:, g, :], h_both[:, g, HI, :], h_both[:, g, LO, :], ALU.add
                                  ).then_inc(h_steps, 1)
                dve.wait_ge(h_steps, before + 3)
                dve.scalar_tensor_tensor(
                    out=h_masked[:, g, :], in0=h_sum[:, g, :], scalar=LORA_SCALE[n],
                    in1=own_batch[:].rearrange("p b s -> p (b s)"), op0=ALU.mult, op1=ALU.mult,
                ).then_inc(h_steps, 1)

            def h_low(q, g):
                for u in range(QUADS):
                    dve.wait_ge(h_hi, QUADS * (GROUPS * q + g) + u + 1)
                    block_of = (quad_rows(u), g, slice(u * QUAD, (u + 1) * QUAD))
                    dve.tensor_tensor(h_parts[LO][block_of], h_masked[quad_rows(u), g, :],
                                      f32(h_parts[HI][block_of]), ALU.subtract).then_inc(h_lo, 1)

            def mask_and_low(n, q):
                for g in range(GROUPS):
                    mask(n, q, g)
                for g in range(GROUPS):
                    h_low(q, g)

            def add_to_x(n, m, tokens, product):
                col = n * SLICES + m
                dve.scalar_tensor_tensor(
                    out=x[:, m, tokens], in0=product, scalar=bias_sb[:, col:col + 1],
                    in1=x[:, m, tokens], op0=ALU.add, op1=ALU.add).then_inc(bank_evicted, 1)

            def evict(n, c, q, banks=out_bank, slices=range(SLICES), done=0):
                for i, m in enumerate(slices):
                    dve.wait_ge(bank_ready, SLICES * q + done + i + 1)
                    add_to_x(n, m, chunk_of(c), banks[m][:])

            for k in range(SLICES):
                dve.wait_ge(w0_landed[k], DMA)
                dve.tensor_copy(w_parts[0][HI][:, k, :, :].rearrange("p m q -> p (m q)"), w_raw[0][:, k, :]
                                ).then_inc(w_hi[0], 1)
                split_w_low(dve, 0, k)
                dve.wait_ge(x_hi[0], k + 1)
                dve.tensor_tensor(x_parts[0][:, LO, k, :], x[:, k, 0:CHUNK],
                                  f32(x_parts[0][:, HI, k, :]), ALU.subtract).then_inc(x_lo[0], 1)

            def a_low(s, g, phases_of_set=0):
                dve.wait_ge(a_hi[s], GROUPS * phases_of_set + g + 1)
                dve.tensor_tensor(a_part(s, LO, g), a_whole(s, g), f32(a_part(s, HI, g)), ALU.subtract
                                  ).then_inc(a_lo[s], 1)

            a_low(0, 0)
            dve.wait_ge(mask_steps, 3)
            dve.tensor_tensor(own_batch[:], own_in_group[:, 0:QUAD_BATCHES, :],
                              own_in_group[:, QUAD_BATCHES:, :], ALU.add).then_inc(mask_steps, 1)
            dve.wait_ge(mask_steps, 4)
            dve.wait_ge(bias_landed, DMA)
            x_low(1, 1, 0)
            a_low(0, 1)
            mask(0, 0, 0)
            h_low(0, 0)
            dve.wait_ge(b_hi[0], 1)
            dve.tensor_tensor(b_parts[0][LO][:], b_raw[0][:, 0:GROUPS, :], f32(b_parts[0][HI][:]),
                              ALU.subtract).then_inc(b_lo[0], 1)
            for g in range(1, GROUPS):
                mask(0, 0, g)
                h_low(0, g)
            a_low(1, 0)
            evict(0, 0, 0, first_bank, FIRST_ORDER[:EARLY])
            a_low(1, 1)
            evict(0, 0, 0, first_bank, FIRST_ORDER[EARLY:], done=EARLY)
            mask(0, 1, 0)
            h_low(1, 0)
            for g in range(1, GROUPS):
                mask(0, 1, g)
                h_low(1, g)
            dve.wait_ge(w_lo[1], W1_EARLY)
            for k in range(W1_EARLY, SLICES):
                split_w_low(dve, 1, k)
            evict(0, 1, 1, slices=range(1))
            x_low(0, 0, 1)
            evict(0, 1, 1, slices=range(1, 2), done=1)
            dve.wait_ge(a_lo[0], 2 * GROUPS - 1)
            a_low(0, GROUPS - 1, 1)
            evict(0, 1, 1, slices=range(2, SLICES), done=2)
            with dve.Fori(0, CHUNKS - 2) as j:
                mask_and_low(1, 2 * j + 2)
                x_low(1, j + 2, j + 1)
                evict(1, j, 2 * j + 2)
                mask_and_low(0, 2 * j + 3)
                x_low(0, j + 1, j + 2)
                evict(0, j + 2, 2 * j + 3)
            mask_and_low(1, 2 * CHUNKS - 2)
            x_low(1, CHUNKS - 1, CHUNKS - 1)
            evict(1, CHUNKS - 2, 2 * CHUNKS - 2)
            mask_and_low(1, 2 * CHUNKS - 1)
            evict(1, CHUNKS - 1, 2 * CHUNKS - 1, slices=range(SLICES - 1))
            for g in range(GROUPS):
                dve.wait_ge(bank_ready, SLICES * 2 * CHUNKS + g)
                add_to_x(1, SLICES - 1, group_of_last_chunk(g),
                         last_bank[g][:, g * GROUP:(g + 1) * GROUP])

        @block.tensor
        def _(pe):
            def base(bank, s, n, m, k, part_of_w, part_of_x, tokens=slice(0, CHUNK)):
                first = k == 0 and (part_of_w, part_of_x) == PASSES[0]
                nc.tensor.matmul(bank[:, tokens], w_parts[n][part_of_w][:, k, m, :],
                                 x_parts[s][:, part_of_x, k, tokens], start=first, stop=False)

            def base_slice(bank, s, n, m, tokens=slice(0, CHUNK), x_parts_before=None):
                for k in range(SLICES):
                    if x_parts_before is not None:
                        pe.wait_ge(x_lo[s], x_parts_before + k + 1)
                    for part_of_w, part_of_x in PASSES:
                        base(bank, s, n, m, k, part_of_w, part_of_x, tokens)

            def lora_down(s, g):
                for u in range(QUADS):
                    quad = g * QUADS + u
                    for k in range(SLICES):
                        last = nc.tensor.matmul(
                            h_bank[g][:, u, :, :], a_parts[s][:, k, quad, :, :].rearrange("p a c -> p (a c)"),
                            x_parts[s][:, :, k, quad * QUAD:(quad + 1) * QUAD],
                            start=(k == 0), stop=(k == SLICES - 1))
                last.then_inc(h_ready, 1)

            def down(s, q, phases_of_set, groups=range(GROUPS)):
                pe.wait_ge(h_steps, H_STEPS * GROUPS * q)
                for g in groups:
                    pe.wait_ge(a_lo[s], GROUPS * phases_of_set + g + 1)
                    lora_down(s, g)

            def lora_up(bank, s, m, g, last_of_bank):
                for i, (part_of_b, part_of_h) in enumerate(PASSES):
                    last = nc.tensor.matmul(
                        bank[:, g * GROUP:(g + 1) * GROUP],
                        b_parts[s][part_of_b][:, g, m * P:(m + 1) * P], h_parts[part_of_h][:, g, :],
                        start=False, stop=(last_of_bank and i == len(PASSES) - 1))
                return last

            def finish_bank(bank, s, m):
                for g in range(GROUPS):
                    last = lora_up(bank, s, m, g, g == GROUPS - 1)
                last.then_inc(bank_ready, 1)

            def wait_lora_rows(s, q, phases_of_set):
                pe.wait_ge(b_lo[s], phases_of_set + 1)
                pe.wait_ge(h_lo, QUADS * GROUPS * (q + 1))

            def up_by_group(banks, s, q, phases_of_set, slices):
                pe.wait_ge(b_lo[s], phases_of_set + 1)
                for g in range(GROUPS):
                    pe.wait_ge(h_lo, QUADS * (GROUPS * q + g + 1))
                    for m in slices:
                        last = lora_up(banks[m], s, m, g, g == GROUPS - 1)
                        if g == GROUPS - 1:
                            last.then_inc(bank_ready, 1)

            def phase(s, n, q, phases_of_set, last_phase=False):
                for m in range(SLICES):
                    pe.wait_ge(bank_evicted, SLICES * (q - 1) + m + 1)
                    if last_phase and m == SLICES - 1:
                        break
                    base_slice(out_bank[m], s, n, m,
                               x_parts_before=SLICES * phases_of_set if m == 0 else None)
                    if m == 0:
                        down(s, q, phases_of_set)
                    if m == LORA_LAG:
                        wait_lora_rows(s, q, phases_of_set)
                        for done in range(m):
                            finish_bank(out_bank[done], s, done)
                    if m >= LORA_LAG:
                        finish_bank(out_bank[m], s, m)

            pe.wait_ge(h_zero, 1)
            for _ in range(WARM_UP):
                nc.tensor.matmul(h_bank[0][:, 0, :, :], h_parts[HI][:, 0, 0:P], h_parts[HI][:, 0, :],
                                 start=True, stop=True)
            for k in range(SLICES):
                pe.wait_ge(w_hi[0], k + 1)
                pe.wait_ge(x_hi[0], k + 1)
                for m in range(SLICES):
                    base(first_bank[m], 0, 0, m, k, HI, HI)
                pe.wait_ge(w_lo[0], k + 1)
                for m in range(SLICES):
                    base(first_bank[m], 0, 0, m, k, LO, HI)
                pe.wait_ge(x_lo[0], k + 1)
                for m in range(SLICES):
                    base(first_bank[m], 0, 0, m, k, HI, LO)
            down(0, 0, 0, [0])
            base_slice(out_bank[0], 1, 0, 0, x_parts_before=0)
            down(0, 0, 0, range(1, GROUPS))
            for m in range(1, EARLY):
                base_slice(out_bank[m], 1, 0, m)
            up_by_group(first_bank, 0, 0, 0, FIRST_ORDER)
            down(1, 1, 0, [0])
            for i, m in enumerate(range(EARLY, SLICES)):
                pe.wait_ge(bank_evicted, i + 1)
                base_slice(out_bank[m], 1, 0, m)
                if i == 0:
                    down(1, 1, 0, range(1, GROUPS))
            up_by_group(out_bank, 1, 1, 0, range(SLICES))
            pe.wait_ge(w_lo[1], SLICES)
            phase(0, 1, 2, 1)
            with pe.Fori(0, CHUNKS - 2) as j:
                phase(1, 0, 2 * j + 3, j + 1)
                phase(0, 1, 2 * j + 4, j + 2)
            phase(1, 1, 2 * CHUNKS - 1, CHUNKS - 1, last_phase=True)
            for g in range(GROUPS):
                base_slice(last_bank[g], 1, 1, SLICES - 1, slice(g * GROUP, (g + 1) * GROUP))
                lora_up(last_bank[g], 1, SLICES - 1, g, True).then_inc(bank_ready, 1)


def kernel(x, itok_B_6_15, itok_B_0_23, L0_cond_base_weight, L0_cond_base_bias, L0_cond_lora_A_w,
           L0_cond_lora_B_w, L1_cond_W, L1_cond_b, L1_cond_lora_As, L1_cond_lora_Bs):
    import numpy as np
    import concourse.bacc as bacc
    from concourse.bass_utils import run_bass_kernel_spmd

    def arr(a):
        return np.ascontiguousarray(np.asarray(a))

    def feature_slices(a):
        a = np.asarray(a)
        return arr(a.reshape(a.shape[:-1] + (P, SLICES)).swapaxes(-1, -2))

    ids = np.stack([np.asarray(itok_B_6_15), np.asarray(itok_B_0_23)])
    by_row = np.repeat(ids.reshape(LAYERS, CHUNKS * GROUPS, GROUP_BATCHES).transpose(2, 0, 1), RANK, axis=0)
    ins = {
        "in_xT": arr(np.asarray(x).reshape(TOKENS, FEATURES).T),
        "in_ids": arr(ids.reshape(1, LAYERS * BATCHES)),
        "in_ids_by_row": arr(by_row.reshape(P, LAYERS * CHUNKS * GROUPS)),
        "in_w0": feature_slices(np.asarray(L0_cond_base_weight).T),
        "in_w1": feature_slices(np.asarray(L1_cond_W).T),
        "in_bias": arr(np.concatenate([np.asarray(L0_cond_base_bias).reshape(P, SLICES),
                                       np.asarray(L1_cond_b).reshape(P, SLICES)], axis=1)),
        "in_a0": arr(np.asarray(L0_cond_lora_A_w).transpose(0, 2, 1)).reshape(ADAPTERS, P, SLICES * RANK),
        "in_a1": arr(L1_cond_lora_As).reshape(ADAPTERS, P, SLICES * RANK),
        "in_b0": feature_slices(np.asarray(L0_cond_lora_B_w).transpose(0, 2, 1)).reshape(
            ADAPTERS * RANK, FEATURES),
        "in_b1": feature_slices(L1_cond_lora_Bs).reshape(ADAPTERS * RANK, FEATURES),
    }
    nc = bacc.Bacc("TRN2", target_bir_lowering=False, num_devices=1)
    t = {name: nc.dram_tensor(name, a.shape, mybir.dt.from_np(a.dtype), kind="ExternalInput").ap()
         for name, a in ins.items()}
    out = nc.dram_tensor("out_yT", (FEATURES, TOKENS), F32, kind="ExternalOutput").ap()
    lora_layers_kernel(nc, t["in_xT"], t["in_ids"], t["in_ids_by_row"], (t["in_w0"], t["in_w1"]),
                       t["in_bias"], (t["in_a0"], t["in_a1"]), (t["in_b0"], t["in_b1"]), out)
    r = run_bass_kernel_spmd(nc, [ins], core_ids=[0])
    return arr(r.results[0]["out_yT"].T).reshape(BATCHES, SEQ, FEATURES)
```
